# Optimizing a Trainium2 kernel written in Bass

```python
import numpy as np
import jax
import jax.numpy as jnp

def _softmax(x, axis=-1):
    return jax.nn.softmax(x, axis=axis)

def _gelu(x):
    return jax.nn.gelu(x, approximate=True)

def _silu(x):
    return jax.nn.silu(x)

def _sigmoid(x):
    return jax.nn.sigmoid(x)

def _layernorm(x, axis=-1, eps=1e-05):
    m = jnp.mean(x, axis=axis, keepdims=True)
    v = jnp.var(x, axis=axis, keepdims=True)
    return (x - m) / jnp.sqrt(v + eps)

def _scatter_add(tgt, idx, src, axis=0):
    return tgt.at[idx].add(src)

def _segment_sum(src, seg, n):
    return jax.ops.segment_sum(src, seg, n)
kernel_name = 'mk_cond_resid_d2_seqx_r2_60581c'

def setup_inputs(seed: int=0):
    np.random.seed(seed)
    _w = jnp.asarray

    def _rec_inputs():
        import jax
        import jax.numpy as jnp
        _rk = jax.random.key(seed)
        x = -7.109e-05 + 0.9999 * jax.random.normal(jax.random.fold_in(_rk, 1), (8, 512, 2048), jnp.float32)
        _lenS = 512 - jax.random.randint(jax.random.fold_in(_rk, 7), (8,), 0, max(1, 512 // 4) + 1, jnp.int32)
        _lenS2 = 512 - jax.random.randint(jax.random.fold_in(_rk, 8), (8,), 0, max(1, 512 // 4) + 1, jnp.int32)
        itok_B_4_50 = jax.random.randint(jax.random.fold_in(_rk, 11), (8,), 4, 51, jnp.int32)
        itok_B_0_23 = jax.random.randint(jax.random.fold_in(_rk, 12), (8,), 0, 24, jnp.int32)
        return (x, itok_B_4_50, itok_B_0_23)
    x, itok_B_4_50, itok_B_0_23 = _rec_inputs()

    def _L0_cond_setup():
        import jax, jax.numpy as jnp
        import numpy as np
        RANK = 16
        ALPHA = 16.0
        SCALING = ALPHA / RANK
        key = jax.random.key(seed)
        k1, k2, k3, k4 = jax.random.split(key, 4)
        batch, n_tok, d_in, d_out, n_adapters, rank = (8, 1024, 2048, 2048, 64, RANK)
        x = jax.random.normal(k1, (batch, n_tok, d_in), dtype=jnp.float32)
        A = jax.random.normal(k2, (n_adapters, d_out, rank), dtype=jnp.float32) * 0.02
        B = jax.random.normal(k3, (n_adapters, rank, d_in), dtype=jnp.float32)
        adapter_ids = jax.random.randint(k4, (batch,), 0, n_adapters, dtype=jnp.int32)
        return {'x': x, 'A': A, 'B': B, 'adapter_ids': adapter_ids}
    _L0_cond_all = _L0_cond_setup()
    _L0_cond_in = {k: v for k, v in _L0_cond_all.items() if k in ('A', 'B')}
    del _L0_cond_all

    def _L1_cond_setup():
        import jax, jax.numpy as jnp
        import numpy as np
        R = 16
        ALPHA = 32
        SCALING = ALPHA / R
        SLOTS = 32
        IN_F = 2048
        OUT_F = 2048
        B, T = (8, 512)
        key = jax.random.key(seed)
        k1, k2, k3, k4, k5, k6 = jax.random.split(key, 6)
        x = jax.random.normal(k1, (B, T, IN_F), dtype=jnp.float32)
        adapter_mapping = jax.random.randint(k2, (B,), 0, SLOTS, dtype=jnp.int32)
        W = jax.random.normal(k3, (OUT_F, IN_F), dtype=jnp.float32) * 0.02
        b = jax.random.normal(k4, (OUT_F,), dtype=jnp.float32) * 0.02
        lora_As = jax.random.normal(k5, (SLOTS, IN_F, R), dtype=jnp.float32) * 0.02
        lora_Bs = jax.random.normal(k6, (SLOTS, R, OUT_F), dtype=jnp.float32) * 0.02
        return {'x': x, 'adapter_mapping': adapter_mapping, 'W': W, 'b': b, 'lora_As': lora_As, 'lora_Bs': lora_Bs}
    _L1_cond_all = _L1_cond_setup()
    _L1_cond_in = {k: v for k, v in _L1_cond_all.items() if k in ('W', 'b', 'lora_As', 'lora_Bs')}
    del _L1_cond_all
    return {'x': x, 'itok_B_4_50': itok_B_4_50, 'itok_B_0_23': itok_B_0_23, 'L0_cond_A': _L0_cond_in['A'], 'L0_cond_B': _L0_cond_in['B'], 'L1_cond_W': _L1_cond_in['W'], 'L1_cond_b': _L1_cond_in['b'], 'L1_cond_lora_As': _L1_cond_in['lora_As'], 'L1_cond_lora_Bs': _L1_cond_in['lora_Bs']}

def reference(x, itok_B_4_50, itok_B_0_23, L0_cond_A, L0_cond_B, L1_cond_W, L1_cond_b, L1_cond_lora_As, L1_cond_lora_Bs):
    import jax
    import jax.numpy as jnp

    def _L0_cond_ref(x, A, B, adapter_ids):
        import jax, jax.numpy as jnp
        import numpy as np
        RANK = 16
        ALPHA = 16.0
        SCALING = ALPHA / RANK
        B_req = B[adapter_ids]
        A_req = A[adapter_ids]
        Bx = jnp.einsum('bni,bri->bnr', x, B_req)
        out = jnp.einsum('bnr,bor->bno', Bx, A_req)
        return out * SCALING

    def _L1_cond_ref(x, adapter_mapping, W, b, lora_As, lora_Bs):
        import jax, jax.numpy as jnp
        import numpy as np
        R = 16
        ALPHA = 32
        SCALING = ALPHA / R
        SLOTS = 32
        IN_F = 2048
        OUT_F = 2048
        B, T = (8, 512)
        base_out = jnp.einsum('bti,oi->bto', x, W) + b
        A = lora_As[adapter_mapping]
        Bm = lora_Bs[adapter_mapping]
        lora_h = jnp.einsum('bti,bir->btr', x, A)
        lora_out = jnp.einsum('btr,bro->bto', lora_h, Bm)
        return base_out + lora_out * SCALING
    x = x + _L0_cond_ref(x, L0_cond_A, L0_cond_B, itok_B_4_50)
    x = x + _L1_cond_ref(x, itok_B_0_23, L1_cond_W, L1_cond_b, L1_cond_lora_As, L1_cond_lora_Bs)
    return x

_drawn_inputs = setup_inputs


def setup_inputs(seed=0):
    import zlib

    import numpy as np

    out = dict(_drawn_inputs(seed))
    spreads = {}
    factors = {'L1_cond_b': 8.0}
    for name, (base, spread) in spreads.items():
        noise = np.random.default_rng([zlib.crc32(name.encode()), seed]).standard_normal(out[name].shape)
        drawn = base * np.exp(spread * noise) if base else spread * noise
        out[name] = jnp.asarray(drawn.astype(out[name].dtype))
    for name, factor in factors.items():
        out[name] = (out[name] * factor).astype(out[name].dtype)
    return out
```

```python
from contextlib import ExitStack

import concourse.bass as bass
from concourse import mybir

F32 = mybir.dt.float32
F32R = mybir.dt.float32r
I32 = mybir.dt.int32
ALU = mybir.AluOpType
ACT = mybir.ActivationFunctionType

P = 128
NB = 8
T = 512
D = 2048
C = D // P
R = 16
REP = P // R
Q = 4
QC = C // Q
SCALE1 = 32.0 / R
XG = 2
XSLOTS = 4
DMA = 16
X_PAIRS = (0, 2)
Y_PAIRS = (3, 7)
PAIRS = C // 2


def build(nc, x, ids0, ids1, a0, b0, w, bias, a1, b1, out):
    with ExitStack() as ctx:
        def sb(name, shape, dt):
            return ctx.enter_context(nc.sbuf_tensor(name, shape, dt))

        def bank(name):
            return ctx.enter_context(nc.psum_tensor(name, [P, T], F32))

        def sem(name):
            return ctx.enter_context(nc.semaphore(name))

        act_hi = [sb(f"act_hi{i}", [P, C, T], F32R) for i in range(2)]
        act_lo = [sb(f"act_lo{i}", [P, C, T], F32R) for i in range(2)]
        x_stage = sb("x_stage", [P, XSLOTS, XG, T], F32)
        y_sum = sb("y_sum", [P, 2, T], F32)
        w_raw = [sb(f"w_raw{i}", [P, C + 1, P], F32) for i in range(2)]
        w_hi = sb("w_hi", [P, C + 1, P], F32R)
        w_lo = sb("w_lo", [P, C, P], F32R)
        down_raw = sb("down_raw", [P, C, R], F32)
        down = sb("down", [P, C, 4, 2, R], F32R)
        up0_raw = sb("up0_raw", [P, D], F32)
        up0 = sb("up0", [P, 2, P], F32R)
        rank0 = sb("rank0", [P, T], F32R)
        rank1 = [sb(f"rank1_{i}", [P, T], F32R) for i in range(2)]
        out_stage = [sb(f"out_stage{i}", [P, T], F32) for i in range(2)]
        bias_sb = sb("bias_sb", [P, C], F32)
        ids_sb = sb("ids_sb", [1, 2, NB], I32)

        acc = [bank(f"acc{i}") for i in range(2)]
        up_ps = [bank(f"up_ps{i}") for i in range(2)]
        down_ps = bank("down_ps")

        ids_loaded = sem("ids_loaded")
        bias_loaded = sem("bias_loaded")
        w_loaded = [sem(f"w_loaded{i}") for i in range(2)]
        x_loaded = [sem(f"x_loaded{i}") for i in range(XSLOTS)]
        down_loaded = sem("down_loaded")
        up0_loaded = sem("up0_loaded")
        w_hi_ready = sem("w_hi_ready")
        w_ready = sem("w_ready")
        quarter_done = sem("quarter_done")
        out_part = sem("out_part")
        out_ready = sem("out_ready")
        out_stored = [sem(f"out_stored{i}") for i in range(2)]
        x_hi_ready = sem("x_hi_ready")
        x_ready = sem("x_ready")
        down_hi_ready = sem("down_hi_ready")
        down_ready = sem("down_ready")
        down_done = sem("down_done")
        rank_hi_ready = sem("rank_hi_ready")
        rank_ready = sem("rank_ready")
        up0_hi_ready = sem("up0_hi_ready")
        up0_ready = sem("up0_ready")
        up0_done = sem("up0_done")
        y_part = sem("y_part")
        y_sum_ready = sem("y_sum_ready")
        y_hi_ready = sem("y_hi_ready")
        y_ready = sem("y_ready")

        block = ctx.enter_context(nc.Block())

        def f32(ap):
            return ap.bitcast(F32)

        def batches(eng, batch):
            with eng.Fori(0, NB // 2 - 1) as i:
                batch(2 * i, 0, True)
                batch(2 * i + 1, 1, True)
            batch(NB - 2, 0, True)
            batch(NB - 1, 1, False)

        @block.sync
        def _(sp):
            def load_w(n, o, s, k, first=False):
                if not first:
                    sp.wait_ge(w_ready, Q * (2 * k + s - 1))
                sp.dma_start(w_raw[s][:, 0:C, :],
                             w[bass.ds(o, 1)].rearrange("u p c f -> (u p) c f")).then_inc(w_loaded[s], DMA)
                a = sp.value_load(ids_sb[0:1, 1, bass.ds(n, 1)], min_val=0, max_val=b1.shape[0] - 1)
                sp.dma_start(
                    w_raw[s][:, C, :],
                    b1[bass.ds(a, 1), bass.ds(o, 1)].rearrange("u v r f -> (u v) r f")
                    .broadcast_to([REP, R, P])).then_inc(w_loaded[s], DMA)

            def load_x(m, g, first=False):
                if not first:
                    sp.wait_ge(x_ready, C * m + XG * (g - XSLOTS + 1))
                sp.dma_start(x_stage[:, g % XSLOTS], x[bass.ds(m, 1), :, XG * g:XG * (g + 1)]
                             .rearrange("u p c t -> (u p) c t")).then_inc(x_loaded[g % XSLOTS], DMA)

            def load_down(m, layer, first=False):
                table = (b0, a1)[layer]
                a = sp.value_load(ids_sb[0:1, layer, bass.ds(m, 1)], min_val=0, max_val=table.shape[0] - 1)
                if not first:
                    sp.wait_ge(down_ready, 2 * m + layer)
                sp.dma_start(down_raw[:, :, :], table[bass.ds(a, 1)].rearrange("u p c r -> (u p) c r"))\
                  .then_inc(down_loaded, DMA)

            def load_up0(m, first=False):
                a = sp.value_load(ids_sb[0:1, 0, bass.ds(m, 1)], min_val=0, max_val=a0.shape[0] - 1)
                if not first:
                    sp.wait_ge(up0_ready, PAIRS * m)
                sp.dma_start(up0_raw[:, :], a0[bass.ds(a, 1)].broadcast_to([REP, R, D]))\
                  .then_inc(up0_loaded, DMA)

            sp.dma_start(ids_sb[:, 0, :], ids0).then_inc(ids_loaded, DMA)
            sp.dma_start(ids_sb[:, 1, :], ids1).then_inc(ids_loaded, DMA)
            for g in range(XSLOTS):
                load_x(0, g, first=True)
            sp.wait_ge(ids_loaded, 2 * DMA)
            load_down(0, 0, first=True)
            load_up0(0, first=True)
            for g in range(XSLOTS, C // XG):
                load_x(0, g)
            load_w(0, 0, 0, 0, first=True)
            load_w(0, 1, 1, 0, first=True)
            load_down(0, 1)
            sp.dma_start(bias_sb[:, :], bias).then_inc(bias_loaded, DMA)
            for g in range(2):
                load_x(1, g)

            def batch(n, par, ahead):
                m = n + 1

                def pair(j, x_groups=((), ()), fresh=False):
                    for s in range(2):
                        if fresh:
                            if ahead:
                                load_w(m, s, s, PAIRS * m)
                        else:
                            load_w(n, 2 * (j + 1) + s, s, PAIRS * n + j + 1)
                        for g in x_groups[s]:
                            load_x(m, g)

                if ahead:
                    load_down(m, 0)
                    load_up0(m)
                    pair(0, ((2, 3), (4, 5)))
                    pair(1, ((6, 7), ()))
                    pair(2)
                    load_down(m, 1)
                    with sp.Fori(Y_PAIRS[0], Y_PAIRS[1]) as j:
                        pair(j)
                else:
                    with sp.Fori(0, PAIRS - 1) as j:
                        pair(j)
                if not ahead:
                    return
                pair(PAIRS - 1, fresh=True)
                if isinstance(n, int):
                    return
                for g in range(2):
                    load_x(n + 2, g)

            batches(sp, batch)

        @block.tensor
        def _(pe):
            def multiply_quarter(t, q, par):
                s = t[1]
                for c in range(QC * q, QC * (q + 1)):
                    pe.matmul(acc[s][:, :], w_hi[:, c, :], act_hi[par][:, c, :], start=(c == 0), stop=False)
                    pe.matmul(acc[s][:, :], w_hi[:, c, :], act_lo[par][:, c, :], start=False, stop=False)
                    mm = pe.matmul(acc[s][:, :], w_lo[:, c, :], act_hi[par][:, c, :],
                                   start=False, stop=(c == C - 1))
                mm.then_inc(quarter_done, 1)

            def step(n, o, s, par, between=None):
                t = C * n + o
                pe.wait_ge(out_part, t + 1)
                for q in range(Q):
                    pe.wait_ge(w_ready, Q * t + q + 1)
                    if q == Q - 1:
                        pe.wait_ge(rank_ready, 2 * n + 2)
                        pe.matmul(acc[s][:, :], w_hi[:, C, :], rank1[par][:, :], start=False, stop=False)
                    multiply_quarter((t, s), q, par)
                    if q == 1 and between:
                        between()

            def down_project(m, layer, par):
                pe.wait_ge(down_ready, 2 * m + layer + 1)
                for c in range(C):
                    if c % QC == 0:
                        pe.wait_ge((x_ready, y_ready)[layer], C * m + c + QC)
                    weights = down[:, c, :, :, :].rearrange("p g h r -> p (g h r)")
                    pe.matmul(down_ps[:, :], weights, act_hi[par][:, c, :], start=(c == 0), stop=False)
                    mm = pe.matmul(down_ps[:, :], weights, act_lo[par][:, c, :], start=False, stop=(c == C - 1))
                mm.then_inc(down_done, 1)

            def up_project(m, k, first=False):
                pe.wait_ge(rank_ready, 2 * m + 1)
                pe.wait_ge(up0_ready, PAIRS * m + k + 1)
                if not first:
                    pe.wait_ge(y_part, C * m + 2 * k)
                for i in range(2):
                    pe.matmul(up_ps[i][:, :], up0[:, i, :], rank0[:, :], start=True, stop=True)\
                      .then_inc(up0_done, 1)

            down_project(0, 0, 0)
            up_project(0, 0, first=True)
            with pe.Fori(1, PAIRS) as k:
                up_project(0, k)
            down_project(0, 1, 0)

            def batch(n, par, ahead):
                m = n + 1

                def pair(j, ups=False):
                    for s in range(2):
                        up = (lambda: up_project(m, 2 * (j - Y_PAIRS[0]) + s)) if ups else None
                        step(n, 2 * j + s, s, par, up)

                def steps_around(j, layer):
                    step(n, 2 * j, 0, par)
                    down_project(m, layer, 1 - par)
                    step(n, 2 * j + 1, 1, par)

                if ahead:
                    with pe.Fori(*X_PAIRS) as j:
                        pair(j)
                    steps_around(2, 0)
                    with pe.Fori(*Y_PAIRS) as j:
                        pair(j, ups=True)
                    steps_around(7, 1)
                else:
                    with pe.Fori(0, PAIRS) as j:
                        pair(j)

            batches(pe, batch)

        @block.scalar
        def _(act):
            def split_w(q, s, k):
                if q == 0:
                    act.wait_ge(w_loaded[s], 2 * DMA * (k + 1))
                end = QC * (q + 1) + (q == Q - 1)
                act.activation(w_hi[:, QC * q:end, :], w_raw[s][:, QC * q:end, :], ACT.Copy)\
                   .then_inc(w_hi_ready, 1)

            def step(n, j, s, auxiliary=(), last=False):
                o = 2 * j + s
                t = C * n + o
                for q in range(Q):
                    if not last:
                        act.wait_ge(quarter_done, Q * t + q + 1)
                        split_w(q, 1 - s, PAIRS * n + j + s)
                    if q < len(auxiliary) and auxiliary[q]:
                        auxiliary[q]()
                act.wait_ge(out_ready, t + 1)
                act.dma_start(out[bass.ds(n, 1), bass.ds(o, 1)].rearrange("u v p t -> (u v p) t"),
                              out_stage[s][:, :]).then_inc(out_stored[s], DMA)

            def split_down(m, layer, first=False):
                d = 2 * m + layer
                act.wait_ge(down_loaded, DMA * (d + 1))
                if not first:
                    act.wait_ge(down_done, d)
                for g in range(4):
                    ins = act.activation(down[:, :, g, 0, :], down_raw[:, :, :], ACT.Copy)
                ins.then_inc(down_hi_ready, 1)

            def split_x(m, c, slot, i, k, par):
                act.wait_ge(x_loaded[slot], DMA * (k + 1))
                act.activation(act_hi[par][:, bass.ds(c, 1), :].rearrange("p u t -> p (u t)"),
                               x_stage[:, slot, i, :], ACT.Copy).then_inc(x_hi_ready, 1)

            def split_rank(m, layer, par):
                dst = (rank0, rank1[par])[layer]
                act.wait_ge(down_done, 2 * m + layer + 1)
                act.activation(dst[:, :], down_ps[:, :], ACT.Copy, scale=(1.0, SCALE1)[layer])\
                   .then_inc(rank_hi_ready, 1)

            def split_up0(m, k, first=False):
                act.wait_ge(up0_loaded, DMA * (m + 1))
                if not first:
                    act.wait_ge(up0_done, C * m + 2 * k)
                act.activation(up0[:, :, :].rearrange("p c f -> p (c f)"),
                               up0_raw[:, bass.ds(2 * P * k, 2 * P)], ACT.Copy).then_inc(up0_hi_ready, 1)

            def split_y(m, k, par):
                for i in range(2):
                    act.wait_ge(y_sum_ready, C * m + 2 * k + i + 1)
                    act.activation(act_hi[par][:, bass.ds(2 * k + i, 1), :].rearrange("p u t -> p (u t)"),
                                   y_sum[:, i, :], ACT.Copy).then_inc(y_hi_ready, 1)

            for s in range(2):
                act.sem_inc(out_stored[s], DMA)
            split_down(0, 0, first=True)
            for c in range(C):
                split_x(0, c, c // XG % XSLOTS, c % XG, c // XG // XSLOTS, 0)
            split_rank(0, 0, 0)
            split_down(0, 1)
            split_up0(0, 0, first=True)
            split_y(0, 0, 0)
            with act.Fori(1, PAIRS) as k:
                split_up0(0, k)
                split_y(0, k, 0)
            for q in range(Q):
                split_w(q, 0, 0)
            split_rank(0, 1, 0)

            def batch(n, par, ahead):
                m, new = n + 1, 1 - par
                loads = C // XG // XSLOTS

                def pair(j, aux=None, last=False):
                    work = aux or (lambda s: ())
                    step(n, j, 0, work(0))
                    step(n, j, 1, work(1), last)

                def x_work(j):
                    def of_step(s):
                        return [(lambda i=i: split_x(m, 8 * j + 4 * s + i,
                                                     2 * s + i // XG, i % XG, loads * m + j, new))
                                for i in range(4)]
                    return of_step

                def y_work(j):
                    def of_step(s):
                        k = 2 * (j - Y_PAIRS[0]) + s
                        return [lambda: split_up0(m, k), None, lambda: split_y(m, k, new)]
                    return of_step

                if not ahead:
                    with act.Fori(0, PAIRS - 1) as j:
                        pair(j)
                    pair(PAIRS - 1, last=True)
                    return
                split_down(m, 0)
                with act.Fori(*X_PAIRS) as j:
                    pair(j, x_work(j))
                step(n, 2, 0)
                split_rank(m, 0, new)
                step(n, 2, 1, (lambda: split_down(m, 1),))
                with act.Fori(*Y_PAIRS) as j:
                    pair(j, y_work(j))
                step(n, 7, 0)
                split_rank(m, 1, new)
                step(n, 7, 1)

            batches(act, batch)
            for s in range(2):
                act.wait_ge(out_stored[s], DMA * (NB * PAIRS + 1))

        @block.vector
        def _(dve):
            def split_w(t, q, s):
                dve.wait_ge(w_hi_ready, Q * t + q + 1)
                if q == Q - 1:
                    for g in (1, 3):
                        rows = slice(32 * g, 32 * (g + 1))
                        dve.tensor_tensor(w_hi[rows, C, :], w_raw[s][rows, C, :], f32(w_hi[rows, C, :]),
                                          ALU.subtract)
                cs = slice(QC * q, QC * (q + 1))
                dve.tensor_tensor(w_lo[:, cs, :], w_raw[s][:, cs, :], f32(w_hi[:, cs, :]), ALU.subtract)\
                   .then_inc(w_ready, 1)

            def half(tile, par, c):
                return tile[par][:, bass.ds(c, 1), :].rearrange("p u t -> p (u t)")

            def finish(n, j, s, par):
                o = 2 * j + s
                t = C * n + o
                dve.wait_ge(quarter_done, Q * (t + 1))
                dve.wait_ge(out_stored[s], DMA * (PAIRS * n + j + 1))
                dve.scalar_tensor_tensor(out=out_stage[s][:, :], in0=acc[s][:, :],
                                         scalar=bias_sb[:, bass.ds(o, 1)], in1=f32(half(act_hi, par, o)),
                                         op0=ALU.add, op1=ALU.add).then_inc(out_part, 1)
                dve.wait_ge(out_part, t + 3)
                dve.tensor_tensor(out_stage[s][:, :], out_stage[s][:, :], f32(half(act_lo, par, o)), ALU.add)\
                   .then_inc(out_ready, 1)

            def step(n, j, s, par, auxiliary=(), last=False):
                t = C * n + 2 * j + s
                for q in range(Q):
                    if not last:
                        split_w(t + 1, q, 1 - s)
                    if q < len(auxiliary) and auxiliary[q]:
                        auxiliary[q]()
                finish(n, j, s, par)

            def split_down(m, layer):
                dve.wait_ge(down_hi_ready, 2 * m + layer + 1)
                for g in range(4):
                    ins = dve.tensor_tensor(down[:, :, g, 1, :], down_raw[:, :, :], f32(down[:, :, g, 0, :]),
                                            ALU.subtract)
                ins.then_inc(down_ready, 1)

            def split_x(m, c, slot, i, par):
                dve.wait_ge(x_hi_ready, C * m + c + 1)
                dve.tensor_tensor(half(act_lo, par, c), x_stage[:, slot, i, :], f32(half(act_hi, par, c)), ALU.subtract)\
                   .then_inc(x_ready, 1)

            def split_rank(m, layer, par):
                dst = (rank0, rank1[par])[layer][P // 2:P, :]
                dve.wait_ge(rank_hi_ready, 2 * m + layer + 1)
                dve.scalar_tensor_tensor(out=dst, in0=down_ps[P // 2:P, :], scalar=(1.0, SCALE1)[layer],
                                         in1=f32(dst), op0=ALU.mult, op1=ALU.subtract)\
                   .then_inc(rank_ready, 1)

            def split_up0(m, k):
                dve.wait_ge(up0_hi_ready, PAIRS * m + k + 1)
                for g in (1, 3):
                    rows = slice(32 * g, 32 * (g + 1))
                    win = up0[rows, :, :].rearrange("p c f -> p (c f)")
                    ins = dve.tensor_tensor(win, up0_raw[rows, bass.ds(2 * P * k, 2 * P)], f32(win),
                                            ALU.subtract)
                ins.then_inc(up0_ready, 1)

            def sum_y(m, k, par):
                for i in range(2):
                    dve.wait_ge(up0_done, C * m + 2 * k + i + 1)
                    dve.tensor_tensor(y_sum[:, i, :], up_ps[i][:, :], f32(half(act_hi, par, 2 * k + i)),
                                      ALU.add).then_inc(y_part, 1)
                for i in range(2):
                    dve.wait_ge(y_part, C * m + 2 * k + i + 1)
                    dve.tensor_tensor(y_sum[:, i, :], y_sum[:, i, :], f32(half(act_lo, par, 2 * k + i)),
                                      ALU.add).then_inc(y_sum_ready, 1)

            def split_y(m, k, par):
                for i in range(2):
                    c = 2 * k + i
                    dve.wait_ge(y_hi_ready, C * m + c + 1)
                    dve.tensor_tensor(half(act_lo, par, c), y_sum[:, i, :], f32(half(act_hi, par, c)),
                                      ALU.subtract).then_inc(y_ready, 1)

            dve.sem_inc(out_part, 2)
            split_down(0, 0)
            for c in range(C):
                split_x(0, c, c // XG % XSLOTS, c % XG, 0)
            split_rank(0, 0, 0)
            split_down(0, 1)
            with dve.Fori(0, PAIRS) as k:
                split_up0(0, k)
                sum_y(0, k, 0)
                split_y(0, k, 0)
            for q in range(Q):
                split_w(0, q, 0)
            split_rank(0, 1, 0)
            dve.wait_ge(bias_loaded, DMA)

            def batch(n, par, ahead):
                m, new = n + 1, 1 - par

                def pair(j, aux=None, last=False):
                    work = aux or (lambda s: ())
                    step(n, j, 0, par, work(0))
                    step(n, j, 1, par, work(1), last)

                def x_work(j):
                    return lambda s: [(lambda i=i: split_x(m, 8 * j + 4 * s + i, 2 * s + i // XG, i % XG, new))
                                      for i in range(4)]

                def y_work(j):
                    def of_step(s):
                        k = 2 * (j - Y_PAIRS[0]) + s
                        return [lambda: split_up0(m, k), None, lambda: sum_y(m, k, new),
                                lambda: split_y(m, k, new)]
                    return of_step

                if not ahead:
                    with dve.Fori(0, PAIRS - 1) as j:
                        pair(j)
                    pair(PAIRS - 1, last=True)
                    return
                split_down(m, 0)
                with dve.Fori(*X_PAIRS) as j:
                    pair(j, x_work(j))
                step(n, 2, 0, par)
                split_rank(m, 0, new)
                step(n, 2, 1, par, (lambda: split_down(m, 1),))
                with dve.Fori(*Y_PAIRS) as j:
                    pair(j, y_work(j))
                step(n, 7, 0, par)
                split_rank(m, 1, new)
                step(n, 7, 1, par)

            batches(dve, batch)


def kernel(x, itok_B_4_50, itok_B_0_23, L0_cond_A, L0_cond_B, L1_cond_W, L1_cond_b,
           L1_cond_lora_As, L1_cond_lora_Bs):
    import numpy as np
    import concourse.bacc as bacc
    from concourse.bass_utils import run_bass_kernel_spmd

    def laid(a, shape, order):
        return np.ascontiguousarray(np.asarray(a).reshape(shape).transpose(order))

    n0, n1 = L0_cond_A.shape[0], L1_cond_lora_As.shape[0]
    arrays = {
        "x": laid(x, (NB, T, C, P), (0, 3, 2, 1)),
        "ids0": laid(itok_B_4_50, (1, NB), (0, 1)),
        "ids1": laid(itok_B_0_23, (1, NB), (0, 1)),
        "a0": laid(L0_cond_A, (n0, D, R), (0, 2, 1)),
        "b0": laid(L0_cond_B, (n0, R, C, P), (0, 3, 2, 1)),
        "w": laid(L1_cond_W, (C, P, C, P), (0, 3, 2, 1)),
        "bias": laid(L1_cond_b, (C, P), (1, 0)),
        "a1": laid(L1_cond_lora_As, (n1, C, P, R), (0, 2, 1, 3)),
        "b1": laid(L1_cond_lora_Bs, (n1, R, C, P), (0, 2, 1, 3)),
    }
    nc = bacc.Bacc("TRN2", target_bir_lowering=False, num_devices=1, dynamic_dma_scratch_size=1024)
    aps = [nc.dram_tensor(name, a.shape, mybir.dt.from_np(a.dtype), kind="ExternalInput").ap()
           for name, a in arrays.items()]
    out = nc.dram_tensor("out", (NB, C, P, T), F32, kind="ExternalOutput").ap()
    build(nc, *aps, out)
    got = run_bass_kernel_spmd(nc, [arrays], core_ids=[0]).results[0]["out"]
    return np.ascontiguousarray(got.transpose(0, 3, 1, 2)).reshape(NB, T, D)
```

```python
from contextlib import ExitStack

import concourse.bass as bass
from concourse import mybir

F32 = mybir.dt.float32
F32R = mybir.dt.float32r
I32 = mybir.dt.int32
ALU = mybir.AluOpType
ACT = mybir.ActivationFunctionType

P = 128
NB = 8
T = 512
D = 2048
C = D // P
R = 16
REP = P // R
Q = 4
QC = C // Q
SCALE1 = 32.0 / R
XG = 2
XSLOTS = 4
DMA = 16
X_PAIRS = 2
Y_PAIR = 3
PAIRS = C // 2


def build(nc, x, ids0, ids1, a0, b0, w, bias, a1, b1, eye, out):
    with ExitStack() as ctx:
        def sb(name, shape, dt):
            return ctx.enter_context(nc.sbuf_tensor(name, shape, dt))

        def bank(name):
            return ctx.enter_context(nc.psum_tensor(name, [P, T], F32))

        def sem(name):
            return ctx.enter_context(nc.semaphore(name))

        act_hi = [sb(f"act_hi{i}", [P, C, T], F32R) for i in range(2)]
        act_lo = [sb(f"act_lo{i}", [P, C, T], F32R) for i in range(2)]
        x_stage = sb("x_stage", [P, XSLOTS, XG, T], F32)
        y_sum = sb("y_sum", [P, 2, T], F32)
        w_raw = [sb(f"w_raw{i}", [P, C + 1, P], F32) for i in range(2)]
        w_hi = sb("w_hi", [P, C + 1, P], F32R)
        w_lo = sb("w_lo", [P, C, P], F32R)
        down_raw = sb("down_raw", [P, C, R], F32)
        down = sb("down", [P, C, 4, 2, R], F32R)
        up0_raw = sb("up0_raw", [P, D], F32)
        up0 = sb("up0", [P, 2, 2, P], F32R)
        identity_raw = sb("identity_raw", [P, P], F32)
        identity = sb("identity", [P, P], F32R)
        rank0 = sb("rank0", [P, T], F32R)
        rank1 = [sb(f"rank1_{i}", [P, T], F32R) for i in range(2)]
        out_stage = [sb(f"out_stage{i}", [P, T], F32) for i in range(2)]
        bias_sb = sb("bias_sb", [P, C], F32)
        ids_sb = sb("ids_sb", [1, 2, NB], I32)

        acc = [bank(f"acc{i}") for i in range(2)]
        up_ps = [bank(f"up_ps{i}") for i in range(2)]
        down_ps = bank("down_ps")

        ids_loaded = sem("ids_loaded")
        bias_loaded = sem("bias_loaded")
        identity_loaded = sem("identity_loaded")
        w_loaded = [sem(f"w_loaded{i}") for i in range(2)]
        x_loaded = [sem(f"x_loaded{i}") for i in range(XSLOTS)]
        down_loaded = sem("down_loaded")
        up0_loaded = sem("up0_loaded")
        w_hi_ready = sem("w_hi_ready")
        w_ready = sem("w_ready")
        quarter_done = sem("quarter_done")
        out_part = sem("out_part")
        out_ready = sem("out_ready")
        out_stored = [sem(f"out_stored{i}") for i in range(2)]
        x_hi_ready = sem("x_hi_ready")
        x_ready = sem("x_ready")
        down_hi_ready = sem("down_hi_ready")
        down_ready = sem("down_ready")
        down_done = sem("down_done")
        rank_hi_ready = sem("rank_hi_ready")
        rank_ready = sem("rank_ready")
        up0_hi_ready = sem("up0_hi_ready")
        up0_ready = sem("up0_ready")
        up0_done = sem("up0_done")
        y_part = sem("y_part")
        y_sum_ready = sem("y_sum_ready")
        y_hi_ready = sem("y_hi_ready")
        y_ready = sem("y_ready")

        block = ctx.enter_context(nc.Block())

        def f32(ap):
            return ap.bitcast(F32)

        def batches(eng, batch):
            with eng.Fori(0, NB // 2 - 1) as i:
                batch(2 * i, 0, True)
                batch(2 * i + 1, 1, True)
            batch(NB - 2, 0, True)
            batch(NB - 1, 1, False)

        @block.sync
        def _(sp):
            def load_w(n, o, s, k, first=False):
                if not first:
                    sp.wait_ge(w_ready, Q * (2 * k + s - 1))
                sp.dma_start(w_raw[s][:, 0:C, :],
                             w[bass.ds(o, 1)].rearrange("u p c f -> (u p) c f")).then_inc(w_loaded[s], DMA)
                a = sp.value_load(ids_sb[0:1, 1, bass.ds(n, 1)], min_val=0, max_val=b1.shape[0] - 1)
                sp.dma_start(
                    w_raw[s][:, C, :],
                    b1[bass.ds(a, 1), bass.ds(o, 1)].rearrange("u v r f -> (u v) r f")
                    .broadcast_to([REP, R, P])).then_inc(w_loaded[s], DMA)

            def load_x(m, g, first=False):
                if not first:
                    sp.wait_ge(x_ready, C * m + XG * (g - XSLOTS + 1))
                sp.dma_start(x_stage[:, g % XSLOTS], x[bass.ds(m, 1), :, XG * g:XG * (g + 1)]
                             .rearrange("u p c t -> (u p) c t")).then_inc(x_loaded[g % XSLOTS], DMA)

            def store(n, j, s):
                t = C * n + 2 * j + s
                sp.wait_ge(out_ready, t + 1)
                sp.dma_start(out[bass.ds(t, 1)].rearrange("u p t -> (u p) t"),
                             out_stage[s][:, :]).then_inc(out_stored[s], DMA)

            def load_down(m, layer, first=False):
                table = (b0, a1)[layer]
                a = sp.value_load(ids_sb[0:1, layer, bass.ds(m, 1)], min_val=0, max_val=table.shape[0] - 1)
                if not first:
                    sp.wait_ge(down_ready, 2 * m + layer)
                sp.dma_start(down_raw[:, :, :], table[bass.ds(a, 1)].rearrange("u p c r -> (u p) c r"))\
                  .then_inc(down_loaded, DMA)

            def load_up0(m, first=False):
                a = sp.value_load(ids_sb[0:1, 0, bass.ds(m, 1)], min_val=0, max_val=a0.shape[0] - 1)
                if not first:
                    sp.wait_ge(up0_ready, PAIRS * m)
                sp.dma_start(up0_raw[:, :], a0[bass.ds(a, 1)].broadcast_to([REP, R, D]))\
                  .then_inc(up0_loaded, DMA)

            sp.dma_start(ids_sb[:, 0, :], ids0).then_inc(ids_loaded, DMA)
            sp.dma_start(ids_sb[:, 1, :], ids1).then_inc(ids_loaded, DMA)
            for g in range(XSLOTS):
                load_x(0, g, first=True)
            sp.dma_start(identity_raw[:, :], eye).then_inc(identity_loaded, DMA)
            sp.wait_ge(ids_loaded, 2 * DMA)
            load_down(0, 0, first=True)
            load_up0(0, first=True)
            for g in range(XSLOTS, C // XG):
                load_x(0, g)
            load_w(0, 0, 0, 0, first=True)
            load_w(0, 1, 1, 0, first=True)
            load_down(0, 1)
            sp.dma_start(bias_sb[:, :], bias).then_inc(bias_loaded, DMA)
            for g in range(2):
                load_x(1, g)
            load_down(1, 0)
            load_up0(1)

            def batch(n, par, ahead):
                m = n + 1

                def pair(j, x_groups=((), ()), fresh=False):
                    for s in range(2):
                        if not fresh:
                            load_w(n, 2 * (j + 1) + s, s, PAIRS * n + j + 1)
                        elif ahead:
                            load_w(m, s, s, PAIRS * m)
                        for g in x_groups[s]:
                            load_x(m, g)
                        store(n, j, s)

                if ahead:
                    pair(0, ((2, 3), (4, 5)))
                    pair(1, ((6, 7), ()))
                    load_down(m, 1)
                    pair(2)
                    with sp.Fori(Y_PAIR, PAIRS - 1) as j:
                        pair(j)
                else:
                    with sp.Fori(0, PAIRS - 1) as j:
                        pair(j)
                more = not isinstance(n, int)
                if more:
                    load_down(n + 2, 0)
                    load_up0(n + 2)
                pair(PAIRS - 1, fresh=True)
                if more:
                    for g in range(2):
                        load_x(n + 2, g)

            for s in range(2):
                sp.sem_inc(out_stored[s], DMA)
            batches(sp, batch)
            for s in range(2):
                sp.wait_ge(out_stored[s], DMA * (NB * PAIRS + 1))

        @block.tensor
        def _(pe):
            def multiply_quarter(t, q, par):
                s = t[1]
                for c in range(QC * q, QC * (q + 1)):
                    pe.matmul(acc[s][:, :], w_hi[:, c, :], act_hi[par][:, c, :], start=(c == 0), stop=False)
                    pe.matmul(acc[s][:, :], w_hi[:, c, :], act_lo[par][:, c, :], start=False, stop=False)
                    mm = pe.matmul(acc[s][:, :], w_lo[:, c, :], act_hi[par][:, c, :],
                                   start=False, stop=(c == C - 1))
                mm.then_inc(quarter_done, 1)

            def step(n, o, s, par, between=None):
                t = C * n + o
                pe.wait_ge(out_part, t + 1)
                for q in range(Q):
                    pe.wait_ge(w_ready, Q * t + q + 1)
                    if q == Q - 1:
                        pe.wait_ge(rank_ready, 2 * n + 2)
                        pe.matmul(acc[s][:, :], w_hi[:, C, :], rank1[par][:, :], start=False, stop=False)
                    multiply_quarter((t, s), q, par)
                    if q == 1 and between:
                        between()

            def down_project(m, layer, par):
                pe.wait_ge(down_ready, 2 * m + layer + 1)
                for c in range(C):
                    if c % QC == 0:
                        pe.wait_ge((x_ready, y_ready)[layer], C * m + c + QC)
                    weights = down[:, c, :, :, :].rearrange("p g h r -> p (g h r)")
                    pe.matmul(down_ps[:, :], weights, act_hi[par][:, c, :], start=(c == 0), stop=False)
                    mm = pe.matmul(down_ps[:, :], weights, act_lo[par][:, c, :], start=False, stop=(c == C - 1))
                mm.then_inc(down_done, 1)

            def up_project(m, i, s):
                k = 2 * i + s
                pe.wait_ge(rank_ready, 2 * m + 1)
                pe.wait_ge(up0_ready, PAIRS * m + k + 1)
                pe.wait_ge(y_part, C * m + 2 * k)
                for u in range(2):
                    pe.matmul(up_ps[u][:, :], up0[:, s, u, :], rank0[:, :], start=True, stop=True)\
                      .then_inc(up0_done, 1)

            def first_up_project(i, s, first=False):
                k = 2 * i + s
                pe.wait_ge(rank_ready, 1)
                pe.wait_ge(up0_ready, k + 1)
                if not first:
                    pe.wait_ge(y_ready, 2 * (k - 1))
                for u in range(2):
                    ps = (up_ps, acc)[s][u]
                    pe.matmul(ps[:, :], up0[:, s, u, :], rank0[:, :], start=True, stop=False)
                    for half in (act_lo, act_hi):
                        mm = pe.matmul(ps[:, :], identity[:, :], half[0][:, bass.ds(2 * k + u, 1), :]
                                       .rearrange("p u t -> p (u t)"), start=False, stop=(half is act_hi))
                    mm.then_inc(up0_done, 1)

            down_project(0, 0, 0)
            for s in range(2):
                first_up_project(0, s, first=True)
            with pe.Fori(1, PAIRS // 2) as i:
                for s in range(2):
                    first_up_project(i, s)
            down_project(0, 1, 0)

            def batch(n, par, ahead):
                m = n + 1

                def pair(j, window=None):
                    for s in range(2):
                        up = None if window is None else lambda: up_project(m, window, s)
                        step(n, 2 * j + s, s, par, up)

                def steps_around(j, layer):
                    step(n, 2 * j, 0, par)
                    down_project(m, layer, 1 - par)
                    step(n, 2 * j + 1, 1, par)

                if ahead:
                    with pe.Fori(0, X_PAIRS) as j:
                        pair(j)
                    steps_around(2, 0)
                    with pe.Fori(0, PAIRS // 2) as i:
                        pair(Y_PAIR + i, window=i)
                    steps_around(7, 1)
                else:
                    with pe.Fori(0, PAIRS) as j:
                        pair(j)

            batches(pe, batch)

        @block.scalar
        def _(act):
            def split_w(q, s, k):
                if q == 0:
                    act.wait_ge(w_loaded[s], 2 * DMA * (k + 1))
                end = QC * (q + 1) + (q == Q - 1)
                act.activation(w_hi[:, QC * q:end, :], w_raw[s][:, QC * q:end, :], ACT.Copy)\
                   .then_inc(w_hi_ready, 1)

            def step(n, j, s, auxiliary=(), last=False):
                o = 2 * j + s
                t = C * n + o
                for q in range(Q):
                    if q < len(auxiliary) and auxiliary[q]:
                        auxiliary[q]()
                    if not last:
                        act.wait_ge(quarter_done, Q * t + q + 1)
                        split_w(q, 1 - s, PAIRS * n + j + s)

            def split_down(m, layer, first=False):
                d = 2 * m + layer
                act.wait_ge(down_loaded, DMA * (d + 1))
                if not first:
                    act.wait_ge(down_done, d)
                for g in range(4):
                    ins = act.activation(down[:, :, g, 0, :], down_raw[:, :, :], ACT.Copy)
                ins.then_inc(down_hi_ready, 1)

            def split_x(m, c, slot, i, k, par):
                act.wait_ge(x_loaded[slot], DMA * (k + 1))
                act.activation(act_hi[par][:, bass.ds(c, 1), :].rearrange("p u t -> p (u t)"),
                               x_stage[:, slot, i, :], ACT.Copy).then_inc(x_hi_ready, 1)

            def split_rank(m, layer, par):
                dst = (rank0, rank1[par])[layer]
                act.wait_ge(down_done, 2 * m + layer + 1)
                act.activation(dst[:, :], down_ps[:, :], ACT.Copy, scale=(1.0, SCALE1)[layer])\
                   .then_inc(rank_hi_ready, 1)

            def split_up0(m, i, s, first=False):
                k = 2 * i + s
                act.wait_ge(up0_loaded, DMA * (m + 1))
                if not first:
                    act.wait_ge(up0_done, C * m + 2 * (k - 1))
                act.activation(up0[:, s, :, :].rearrange("p c f -> p (c f)"),
                               up0_raw[:, bass.ds(2 * P * k, 2 * P)], ACT.Copy).then_inc(up0_hi_ready, 1)

            def split_y(m, i, s, par):
                for u in range(2):
                    c = 4 * i + 2 * s + u
                    act.wait_ge(y_sum_ready, C * (m - 1) + c + 1)
                    act.activation(act_hi[par][:, bass.ds(c, 1), :].rearrange("p u t -> p (u t)"),
                                   y_sum[:, u, :], ACT.Copy).then_inc(y_hi_ready, 1)

            def first_split_y(i, s):
                for u in range(2):
                    c = 4 * i + 2 * s + u
                    act.wait_ge(up0_done, c + 1)
                    act.activation(act_hi[0][:, bass.ds(c, 1), :].rearrange("p u t -> p (u t)"),
                                   (up_ps, acc)[s][u][:, :], ACT.Copy).then_inc(y_hi_ready, 1)

            split_down(0, 0, first=True)
            for c in range(C):
                split_x(0, c, c // XG % XSLOTS, c % XG, c // XG // XSLOTS, 0)
            split_rank(0, 0, 0)
            split_down(0, 1)
            act.wait_ge(identity_loaded, DMA)
            act.activation(identity[:, :], identity_raw[:, :], ACT.Copy)
            for s in range(2):
                split_up0(0, 0, s, first=True)
            for s in range(2):
                first_split_y(0, s)
            with act.Fori(1, PAIRS // 2) as i:
                for s in range(2):
                    split_up0(0, i, s)
                    first_split_y(i, s)
            for q in range(Q):
                split_w(q, 0, 0)
            split_rank(0, 1, 0)

            def batch(n, par, ahead):
                m, new = n + 1, 1 - par
                loads = C // XG // XSLOTS

                def pair(j, aux=None, last=False):
                    work = aux or (lambda s: ())
                    step(n, j, 0, work(0))
                    step(n, j, 1, work(1), last)

                def x_work(j):
                    def of_step(s):
                        return [(lambda i=i: split_x(m, 8 * j + 4 * s + i,
                                                     2 * s + i // XG, i % XG, loads * m + j, new))
                                for i in range(4)]
                    return of_step

                def y_work(i):
                    def of_step(s):
                        return [lambda: split_up0(m, i, s), None, None, lambda: split_y(m, i, s, new)]
                    return of_step

                if not ahead:
                    with act.Fori(0, PAIRS - 1) as j:
                        pair(j)
                    pair(PAIRS - 1, last=True)
                    return
                split_down(m, 0)
                with act.Fori(0, X_PAIRS) as j:
                    pair(j, x_work(j))
                step(n, 2, 0)
                split_rank(m, 0, new)
                step(n, 2, 1, (lambda: split_down(m, 1),))
                with act.Fori(0, PAIRS // 2) as i:
                    pair(Y_PAIR + i, y_work(i))
                step(n, 7, 0)
                split_rank(m, 1, new)
                step(n, 7, 1)

            batches(act, batch)

        @block.vector
        def _(dve):
            def split_w(t, q, s):
                dve.wait_ge(w_hi_ready, Q * t + q + 1)
                if q == Q - 1:
                    for g in (1, 3):
                        rows = slice(32 * g, 32 * (g + 1))
                        dve.tensor_tensor(w_hi[rows, C, :], w_raw[s][rows, C, :], f32(w_hi[rows, C, :]),
                                          ALU.subtract)
                cs = slice(QC * q, QC * (q + 1))
                dve.tensor_tensor(w_lo[:, cs, :], w_raw[s][:, cs, :], f32(w_hi[:, cs, :]), ALU.subtract)\
                   .then_inc(w_ready, 1)

            def half(tile, par, c):
                return tile[par][:, bass.ds(c, 1), :].rearrange("p u t -> p (u t)")

            def finish(n, j, s, par):
                o = 2 * j + s
                t = C * n + o
                dve.wait_ge(quarter_done, Q * (t + 1))
                dve.wait_ge(out_stored[s], DMA * (PAIRS * n + j + 1))
                dve.scalar_tensor_tensor(out=out_stage[s][:, :], in0=acc[s][:, :],
                                         scalar=bias_sb[:, bass.ds(o, 1)], in1=f32(half(act_hi, par, o)),
                                         op0=ALU.add, op1=ALU.add).then_inc(out_part, 1)
                dve.wait_ge(out_part, t + 3)
                dve.tensor_tensor(out_stage[s][:, :], out_stage[s][:, :], f32(half(act_lo, par, o)), ALU.add)\
                   .then_inc(out_ready, 1)

            def step(n, j, s, par, auxiliary=(), last=False):
                t = C * n + 2 * j + s
                for q in range(Q):
                    if q < len(auxiliary) and auxiliary[q]:
                        auxiliary[q]()
                    if not last:
                        split_w(t + 1, q, 1 - s)
                finish(n, j, s, par)

            def split_down(m, layer):
                dve.wait_ge(down_hi_ready, 2 * m + layer + 1)
                for g in range(4):
                    ins = dve.tensor_tensor(down[:, :, g, 1, :], down_raw[:, :, :], f32(down[:, :, g, 0, :]),
                                            ALU.subtract)
                ins.then_inc(down_ready, 1)

            def split_x(m, c, slot, i, par):
                dve.wait_ge(x_hi_ready, C * m + c + 1)
                dve.tensor_tensor(half(act_lo, par, c), x_stage[:, slot, i, :], f32(half(act_hi, par, c)), ALU.subtract)\
                   .then_inc(x_ready, 1)

            def split_rank(m, layer, par):
                dst = (rank0, rank1[par])[layer][P // 2:P, :]
                dve.wait_ge(rank_hi_ready, 2 * m + layer + 1)
                dve.scalar_tensor_tensor(out=dst, in0=down_ps[P // 2:P, :], scalar=(1.0, SCALE1)[layer],
                                         in1=f32(dst), op0=ALU.mult, op1=ALU.subtract)\
                   .then_inc(rank_ready, 1)

            def split_up0(m, i, s):
                k = 2 * i + s
                dve.wait_ge(up0_hi_ready, PAIRS * m + k + 1)
                for g in (1, 3):
                    rows = slice(32 * g, 32 * (g + 1))
                    win = up0[rows, s, :, :].rearrange("p c f -> p (c f)")
                    ins = dve.tensor_tensor(win, up0_raw[rows, bass.ds(2 * P * k, 2 * P)], f32(win),
                                            ALU.subtract)
                ins.then_inc(up0_ready, 1)

            def sum_y(m, i, s, par):
                for u in range(2):
                    c = 4 * i + 2 * s + u
                    dve.wait_ge(up0_done, C * m + c + 1)
                    dve.tensor_tensor(y_sum[:, u, :], up_ps[u][:, :], f32(half(act_hi, par, c)),
                                      ALU.add).then_inc(y_part, 1)
                for u in range(2):
                    c = 4 * i + 2 * s + u
                    dve.wait_ge(y_part, C * m + c + 1)
                    dve.tensor_tensor(y_sum[:, u, :], y_sum[:, u, :], f32(half(act_lo, par, c)),
                                      ALU.add).then_inc(y_sum_ready, 1)

            def split_y(m, i, s, par):
                for u in range(2):
                    c = 4 * i + 2 * s + u
                    dve.wait_ge(y_hi_ready, C * m + c + 1)
                    dve.tensor_tensor(half(act_lo, par, c), y_sum[:, u, :], f32(half(act_hi, par, c)),
                                      ALU.subtract).then_inc(y_ready, 1)

            def first_split_y(i, s):
                for u in range(2):
                    c = 4 * i + 2 * s + u
                    dve.wait_ge(y_hi_ready, c + 1)
                    dve.tensor_tensor(half(act_lo, 0, c), (up_ps, acc)[s][u][:, :], f32(half(act_hi, 0, c)),
                                      ALU.subtract).then_inc(y_ready, 1)

            dve.sem_inc(out_part, 2)
            dve.sem_inc(y_part, C)
            split_down(0, 0)
            for c in range(C):
                split_x(0, c, c // XG % XSLOTS, c % XG, 0)
            split_rank(0, 0, 0)
            split_down(0, 1)
            for s in range(2):
                split_up0(0, 0, s)
            for s in range(2):
                first_split_y(0, s)
            with dve.Fori(1, PAIRS // 2) as i:
                for s in range(2):
                    split_up0(0, i, s)
                    first_split_y(i, s)
            for q in range(Q):
                split_w(0, q, 0)
            split_rank(0, 1, 0)
            dve.wait_ge(bias_loaded, DMA)

            def batch(n, par, ahead):
                m, new = n + 1, 1 - par

                def pair(j, aux=None, last=False):
                    work = aux or (lambda s: ())
                    step(n, j, 0, par, work(0))
                    step(n, j, 1, par, work(1), last)

                def x_work(j):
                    return lambda s: [(lambda i=i: split_x(m, 8 * j + 4 * s + i, 2 * s + i // XG, i % XG, new))
                                      for i in range(4)]

                def y_work(i):
                    def of_step(s):
                        return [lambda: split_up0(m, i, s), None, lambda: sum_y(m, i, s, new),
                                lambda: split_y(m, i, s, new)]
                    return of_step

                if not ahead:
                    with dve.Fori(0, PAIRS - 1) as j:
                        pair(j)
                    pair(PAIRS - 1, last=True)
                    return
                split_down(m, 0)
                with dve.Fori(0, X_PAIRS) as j:
                    pair(j, x_work(j))
                step(n, 2, 0, par)
                split_rank(m, 0, new)
                step(n, 2, 1, par, (lambda: split_down(m, 1),))
                with dve.Fori(0, PAIRS // 2) as i:
                    pair(Y_PAIR + i, y_work(i))
                step(n, 7, 0, par)
                split_rank(m, 1, new)
                step(n, 7, 1, par)

            batches(dve, batch)


def kernel(x, itok_B_4_50, itok_B_0_23, L0_cond_A, L0_cond_B, L1_cond_W, L1_cond_b,
           L1_cond_lora_As, L1_cond_lora_Bs):
    import numpy as np
    import concourse.bacc as bacc
    from concourse.bass_utils import run_bass_kernel_spmd

    def laid(a, shape, order):
        return np.ascontiguousarray(np.asarray(a).reshape(shape).transpose(order))

    n0, n1 = L0_cond_A.shape[0], L1_cond_lora_As.shape[0]
    arrays = {
        "x": laid(x, (NB, T, C, P), (0, 3, 2, 1)),
        "ids0": laid(itok_B_4_50, (1, NB), (0, 1)),
        "ids1": laid(itok_B_0_23, (1, NB), (0, 1)),
        "a0": laid(L0_cond_A, (n0, D, R), (0, 2, 1)),
        "b0": laid(L0_cond_B, (n0, R, C, P), (0, 3, 2, 1)),
        "w": laid(L1_cond_W, (C, P, C, P), (0, 3, 2, 1)),
        "bias": laid(L1_cond_b, (C, P), (1, 0)),
        "a1": laid(L1_cond_lora_As, (n1, C, P, R), (0, 2, 1, 3)),
        "b1": laid(L1_cond_lora_Bs, (n1, R, C, P), (0, 2, 1, 3)),
        "eye": np.eye(P, dtype=np.float32),
    }
    nc = bacc.Bacc("TRN2", target_bir_lowering=False, num_devices=1, dynamic_dma_scratch_size=1024)
    aps = [nc.dram_tensor(name, a.shape, mybir.dt.from_np(a.dtype), kind="ExternalInput").ap()
           for name, a in arrays.items()]
    out = nc.dram_tensor("out", (NB * C, P, T), F32, kind="ExternalOutput").ap()
    build(nc, *aps, out)
    got = run_bass_kernel_spmd(nc, [arrays], core_ids=[0]).results[0]["out"]
    return np.ascontiguousarray(got.reshape(NB, C, P, T).transpose(0, 3, 1, 2)).reshape(NB, T, D)
```
